# Optimizing a Trainium2 kernel written in Bass

```python
import numpy as np
import jax
import jax.numpy as jnp

def _softmax(x, axis=-1):
    return jax.nn.softmax(x, axis=axis)

def _gelu(x):
    return jax.nn.gelu(x, approximate=True)

def _silu(x):
    return jax.nn.silu(x)

def _sigmoid(x):
    return jax.nn.sigmoid(x)

def _layernorm(x, axis=-1, eps=1e-05):
    m = jnp.mean(x, axis=axis, keepdims=True)
    v = jnp.var(x, axis=axis, keepdims=True)
    return (x - m) / jnp.sqrt(v + eps)

def _scatter_add(tgt, idx, src, axis=0):
    return tgt.at[idx].add(src)

def _segment_sum(src, seg, n):
    return jax.ops.segment_sum(src, seg, n)
kernel_name = 'mk_sandwich_d1_jaxref_r8_ff4c01'

def setup_inputs(seed: int=0):
    np.random.seed(seed)
    _w = jnp.asarray

    def _L0_attn_setup():
        import jax, jax.numpy as jnp
        import numpy as np
        B, S, EMB = (2, 256, 512)
        NHEADS, KVHEADS, HEAD_D = (32, 8, 128)
        SPLITS = (NHEADS * HEAD_D, KVHEADS * HEAD_D, KVHEADS * HEAD_D)
        key = jax.random.key(seed)
        k1, k2, k3 = jax.random.split(key, 3)
        q = jax.random.normal(k1, (B, S, EMB), dtype=jnp.float32)
        w_qkv = jax.random.normal(k2, (sum(SPLITS), EMB), dtype=jnp.float32) * 0.02
        w_dense = jax.random.normal(k3, (EMB, NHEADS * HEAD_D), dtype=jnp.float32) * 0.02
        return {'q': q, 'w_qkv': w_qkv, 'w_dense': w_dense}
    _L0_attn_in = _L0_attn_setup()

    def _L0_ffn_setup():
        import jax, jax.numpy as jnp
        import numpy as np
        BS = 128
        FP8_MAX = 448.0

        def act_quant(x):
            T, K = x.shape
            xb = x.reshape(T, K // BS, BS)
            amax = jnp.max(jnp.abs(xb), axis=-1)
            scale = amax / FP8_MAX + 1e-12
            xq = (xb / scale[:, :, None]).reshape(T, K)
            return (xq, scale)

        def linear_dsv3(x, wq, w_scale):
            T, K = x.shape
            N = wq.shape[0]
            xq, xs = act_quant(x)
            xdq = (xq.reshape(T, K // BS, BS) * xs[:, :, None]).reshape(T, K)
            wdq = (wq.reshape(N // BS, BS, K // BS, BS) * w_scale[:, None, :, None]).reshape(N, K)
            return xdq @ wdq.T
        key = jax.random.key(seed)
        ks = jax.random.split(key, 4)
        DIM, INTER = (512, 1792)

        def make_qweight(k, n, m):
            w = jax.random.normal(k, (n, m), dtype=jnp.float32) * 0.02
            wb = w.reshape(n // BS, BS, m // BS, BS)
            amax = jnp.max(jnp.abs(wb), axis=(1, 3))
            scale = amax / FP8_MAX + 1e-12
            wq = (wb / scale[:, None, :, None]).reshape(n, m)
            return (wq, scale)
        x = jax.random.normal(ks[0], (2, 128, DIM), dtype=jnp.float32)
        w1, w1_scale = make_qweight(ks[1], INTER, DIM)
        w3, w3_scale = make_qweight(ks[2], INTER, DIM)
        w2, w2_scale = make_qweight(ks[3], DIM, INTER)
        return {'x': x, 'w1': w1, 'w1_scale': w1_scale, 'w3': w3, 'w3_scale': w3_scale, 'w2': w2, 'w2_scale': w2_scale}
    _L0_ffn_in = _L0_ffn_setup()
    _d = {'L0_attn_q': _L0_attn_in['q'], 'L0_attn_w_qkv': _L0_attn_in['w_qkv'], 'L0_attn_w_dense': _L0_attn_in['w_dense'], 'L0_ffn_w1': _L0_ffn_in['w1'], 'L0_ffn_w1_scale': _L0_ffn_in['w1_scale'], 'L0_ffn_w3': _L0_ffn_in['w3'], 'L0_ffn_w3_scale': _L0_ffn_in['w3_scale'], 'L0_ffn_w2': _L0_ffn_in['w2'], 'L0_ffn_w2_scale': _L0_ffn_in['w2_scale']}
    _x0 = _d['L0_attn_q']
    _d['L0_attn_q'] = jax.random.normal(jax.random.fold_in(jax.random.key(seed), 1), (1, 1024, 512), dtype=_x0.dtype)
    del _x0
    return _d

def reference(L0_attn_q, L0_attn_w_qkv, L0_attn_w_dense, L0_ffn_w1, L0_ffn_w1_scale, L0_ffn_w3, L0_ffn_w3_scale, L0_ffn_w2, L0_ffn_w2_scale):

    def _L0_attn_ref(q, w_qkv, w_dense):
        import jax, jax.numpy as jnp
        import numpy as np
        B, S, EMB = (2, 256, 512)
        NHEADS, KVHEADS, HEAD_D = (32, 8, 128)
        SPLITS = (NHEADS * HEAD_D, KVHEADS * HEAD_D, KVHEADS * HEAD_D)
        Bq, Sq, _ = q.shape
        qkv = q @ w_qkv.T
        qs, ks, vs = jnp.split(qkv, np.cumsum(SPLITS)[:-1], axis=-1)
        G = NHEADS // KVHEADS
        qh = qs.reshape(Bq, Sq, KVHEADS, G, HEAD_D)
        kh = ks.reshape(Bq, Sq, KVHEADS, HEAD_D)
        vh = vs.reshape(Bq, Sq, KVHEADS, HEAD_D)
        scale = 1.0 / jnp.sqrt(jnp.float32(HEAD_D))
        scores = jnp.einsum('bskgd,btkd->bkgst', qh, kh) * scale
        causal = jnp.tril(jnp.ones((Sq, Sq), dtype=bool))
        scores = jnp.where(causal, scores, jnp.finfo(scores.dtype).min)
        probs = jax.nn.softmax(scores, axis=-1)
        attn = jnp.einsum('bkgst,btkd->bskgd', probs, vh)
        attn = attn.reshape(Bq, Sq, NHEADS * HEAD_D)
        return attn @ w_dense.T

    def _L0_ffn_ref(x, w1, w1_scale, w3, w3_scale, w2, w2_scale):
        import jax, jax.numpy as jnp
        import numpy as np
        BS = 128
        FP8_MAX = 448.0

        def act_quant(x):
            T, K = x.shape
            xb = x.reshape(T, K // BS, BS)
            amax = jnp.max(jnp.abs(xb), axis=-1)
            scale = amax / FP8_MAX + 1e-12
            xq = (xb / scale[:, :, None]).reshape(T, K)
            return (xq, scale)

        def linear_dsv3(x, wq, w_scale):
            T, K = x.shape
            N = wq.shape[0]
            xq, xs = act_quant(x)
            xdq = (xq.reshape(T, K // BS, BS) * xs[:, :, None]).reshape(T, K)
            wdq = (wq.reshape(N // BS, BS, K // BS, BS) * w_scale[:, None, :, None]).reshape(N, K)
            return xdq @ wdq.T
        B, S, D = x.shape
        xf = x.reshape(-1, D)
        g = linear_dsv3(xf, w1, w1_scale)
        u = linear_dsv3(xf, w3, w3_scale)
        h = jax.nn.silu(g) * u
        y = linear_dsv3(h, w2, w2_scale)
        return y.reshape(B, S, D)
    x = L0_attn_q
    x = x + _layernorm(_L0_attn_ref(_layernorm(x, axis=-1), L0_attn_w_qkv, L0_attn_w_dense), axis=-1)
    x = x + _layernorm(_L0_ffn_ref(_layernorm(x, axis=-1), L0_ffn_w1, L0_ffn_w1_scale, L0_ffn_w3, L0_ffn_w3_scale, L0_ffn_w2, L0_ffn_w2_scale), axis=-1)
    return x

_drawn_inputs = setup_inputs


def setup_inputs(seed=0):
    import zlib

    import numpy as np

    out = dict(_drawn_inputs(seed))
    spreads = {}
    factors = {}
    for name, (base, spread) in spreads.items():
        noise = np.random.default_rng([zlib.crc32(name.encode()), seed]).standard_normal(out[name].shape)
        drawn = base * np.exp(spread * noise) if base else spread * noise
        out[name] = jnp.asarray(drawn.astype(out[name].dtype))
    for name, factor in factors.items():
        out[name] = (out[name] * factor).astype(out[name].dtype)
    return out
```

```python
from contextlib import ExitStack

import concourse.bass as bass
from concourse import mybir

F32 = mybir.dt.float32
F32R = mybir.dt.float32r
ALU = mybir.AluOpType
ACT = mybir.ActivationFunctionType
AXX = mybir.AxisListType.X

P = 128
BANK = 512
NEG = -1.0e38
EPS = 1e-5
FP8_MAX = 448.0
SCALE_FLOOR = 1e-12


def sandwich_kernel(nc, x, w_attn, w_dense, w_up, w_down, s_up, s_down, out):
    S, D = x.shape
    G = w_attn.shape[0]
    KT = D // P
    WC = w_attn.shape[3]
    HG = WC // P - 2
    NT = S // P
    NH = S // BANK
    C = w_up.shape[0]
    CW = w_up.shape[3] // 2
    CB = CW // P
    SCALE = float(P) ** -0.5
    K_COL, V_COL = HG * P, (HG + 1) * P
    TPB = BANK // P
    assert D == BANK and HG == TPB and HG * P == D and C % 2 == 1 and 2 * CW == BANK and NH == 2

    T_PRO = NT
    T_K = [0, HG + 2]
    T_VT = [1, HG + 3]
    T_Q = [2, HG + 4 + NH]
    T_V = HG + 4
    T_P = [T_Q[1] + HG]
    for i in range(NT):
        T_P.append(T_P[-1] + HG * ((i + TPB) // TPB))
    T_GROUP = T_P[NT]
    T_ATT = T_PRO + G * T_GROUP
    assert T_PRO % 2 == 0 and T_GROUP % 2 == 0
    H_GROUP = T_GROUP - NH

    def hi_count(k):
        return k + 1 - sum(k > u for u in T_VT)

    def p_banks(i):
        return (i + TPB) // TPB

    def p_use(i, h, b):
        return T_P[i] + h * p_banks(i) + b

    with ExitStack() as ctx:
        def sb(name, shape, dt=F32):
            return ctx.enter_context(nc.sbuf_tensor(name, shape, dt))

        def sem(name):
            return ctx.enter_context(nc.semaphore(name))

        xnT = [sb(f"xnT_{p}", [P, KT, S], F32R) for p in ("hi", "lo")]
        w = [sb(f"w_{p}", [P, KT, WC], F32R) for p in ("hi", "lo")]
        qT = [sb(f"qT_{p}", [P, HG, S], F32R) for p in ("hi", "lo")]
        kT = [sb(f"kT_{p}", [P, S], F32R) for p in ("hi", "lo")]
        v = [sb(f"v_{p}", [P, NT, P], F32R) for p in ("hi", "lo")]
        wd = [sb(f"wd_{p}", [P, HG, D], F32R) for p in ("hi", "lo")]
        pT = [sb(f"pT_{p}", [P, NT, BANK], F32R) for p in ("hi", "lo")]
        oT = [sb(f"oT_{p}", [P, BANK], F32R) for p in ("hi", "lo")]
        probs = sb("probs", [P, HG, S])
        xt = probs[:].rearrange("p h (u d) -> p (h u) d", d=D)
        y = sb("y", [P, NT, D])
        raw = sb("raw", [P, KT * WC])
        mask = sb("mask", [P, S])
        ident = sb("ident", [P, P])
        s_up_b = sb("s_up_b", [P, s_up.shape[1]])
        s_down_b = sb("s_down_b", [P, s_down.shape[1]])
        negmax = sb("negmax", [P, HG])
        lsum = sb("lsum", [P, HG])
        rsum = sb("rsum", [P, HG])
        st = sb("st", [P, NT, 6])
        mv = sb("mv", [P, NT, 2])
        mv1 = sb("mv1", [P, NT, 2])
        rstd = sb("rstd", [P, NT])
        rstd1 = sb("rstd1", [P, NT])
        half = sb("half", [P, 1])
        amax = sb("amax", [P, 2, KT])
        qs = sb("qs", [P, 2, KT])
        qr = sb("qr", [P, 2, KT])
        hmax = sb("hmax", [P, 2, CB])
        hs = sb("hs", [P, 2, CB])
        hr = sb("hr", [P, 2, CB])
        g_sb = mask[:, 0:2 * CW].rearrange("p (s c) -> p s c", s=2)
        h_sb = mask[:, 2 * CW:4 * CW].rearrange("p (s c) -> p s c", s=2)

        raw_w = raw[:].rearrange("p (k c) -> p k c", k=KT)
        raw_wd = raw[:, 0:HG * D].rearrange("p (h d) -> p h d", h=HG)
        UPC = KT * 2 * CW
        raw_up = raw[:, 0:UPC].rearrange("p (k c) -> p k c", k=KT)
        raw_down = raw[:, UPC:UPC + CB * D].rearrange("p (k d) -> p k d", k=CB)

        psS = ctx.enter_context(nc.psum_tensor("psS", [P, 2, S], F32))
        psT = ctx.enter_context(nc.psum_tensor("psT", [P, 2, BANK], F32))
        psOY = ctx.enter_context(nc.psum_tensor("psOY", [P, 2, BANK], F32))
        psO, psY = psOY[:, 0, :], psOY[:, 1, :]

        x_in = [sem(f"x_in{i}") for i in range(NT)]
        scales_in = sem("scales_in")
        w_in = sem("w_in")
        wd_in = sem("wd_in")
        ffn_in = sem("ffn_in")
        out_done = sem("out_done")
        raw_free = sem("raw_free")
        const_ready = sem("const_ready")
        pool_passed = sem("pool_passed")
        dve_passed = sem("dve_passed")
        pool_step = sem("pool_step")
        w_ready = sem("w_ready")
        wd_ready = sem("wd_ready")
        stat_x, stat_y, stat_x1, stat_fin = (sem(f"stat_{n}") for n in ("x", "y", "x1", "fin"))
        rstd_x, rstd_y, rstd_x1, rstd_fin = (sem(f"rstd_{n}") for n in ("x", "y", "x1", "fin"))
        own_step = sem("own_step")
        xn_ready = sem("xn_ready")
        xn1_ready = sem("xn1_ready")
        t_full = sem("t_full")
        t_hi = sem("t_hi")
        t_done = sem("t_done")
        s_full = sem("s_full")
        s_done = sem("s_done")
        e_done = sem("e_done")
        r_done = sem("r_done")
        p_ready = sem("p_ready")
        o_full = sem("o_full")
        o_hi = sem("o_hi")
        o_done = sem("o_done")
        y_full = sem("y_full")
        y_done = sem("y_done")
        scaled = sem("scaled")
        up_ready = sem("up_ready")
        down_ready = sem("down_ready")
        gu_full = sem("gu_full")
        g_done = sem("g_done")
        h_made = sem("h_made")
        h_step = sem("h_step")
        h_scaled = sem("h_scaled")
        h_ready = sem("h_ready")
        ht_full = sem("ht_full")
        ht_hi = sem("ht_hi")
        ht_done = sem("ht_done")
        d_full = sem("d_full")
        d_done = sem("d_done")
        z_ready = sem("z_ready")
        fin_ready = sem("fin_ready")

        block = ctx.enter_context(nc.Block())

        def split_passes(a, b):
            (a_hi, a_lo), (b_hi, b_lo) = a, b
            return [(a_hi, b_hi), (a_hi, b_lo), (a_lo, b_hi)]

        @block.sync
        def _(sp):
            sp.dma_start(xt[:, 0, :], x[0:P, :]).then_inc(x_in[0], 16)
            sp.dma_start(xt[:, 1, :], x[P:2 * P, :]).then_inc(x_in[1], 16)
            sp.dma_start(raw_w, w_attn[0]).then_inc(w_in, 16)
            for i in range(2, NT):
                sp.dma_start(xt[:, i, :], x[i * P:(i + 1) * P, :]).then_inc(x_in[i], 16)
            for table, source in ((s_up_b, s_up), (s_down_b, s_down)):
                sp.dma_start(table[:], source.broadcast_to([P, source.shape[1]])).then_inc(scales_in, 16)
            sp.wait_ge(raw_free, 1)
            sp.dma_start(raw_wd, w_dense[0]).then_inc(wd_in, 16)
            with sp.Fori(0, G - 1) as g:
                sp.wait_ge(raw_free, 2 * g + 2)
                sp.dma_start(raw_w, w_attn[g + 1]).then_inc(w_in, 16)
                sp.wait_ge(raw_free, 2 * g + 3)
                sp.dma_start(raw_wd, w_dense[g + 1]).then_inc(wd_in, 16)
            sp.wait_ge(raw_free, 2 * G)
            sp.dma_start(raw_up, w_up[0]).then_inc(ffn_in, 16)
            sp.dma_start(raw_down, w_down[0]).then_inc(ffn_in, 16)
            sp.wait_ge(t_full, T_ATT)
            for i in range(NT):
                sp.dma_start(xt[:, i, :], x[i * P:(i + 1) * P, :]).then_inc(x_in[i], 16)
            with sp.Fori(1, C) as c:
                sp.wait_ge(raw_free, 2 * G + c)
                sp.dma_start(raw_up, w_up[c]).then_inc(ffn_in, 16)
                sp.dma_start(raw_down, w_down[c]).then_inc(ffn_in, 16)
            for i in range(NT):
                sp.wait_ge(fin_ready, i + 1)
                sp.dma_start(out[i * P:(i + 1) * P, :], xt[:, i, :]).then_inc(out_done, 16)
            sp.wait_ge(out_done, 16 * NT)

        @block.gpsimd
        def _(pool):
            STEP_GROUP = HG + KT
            STEP_FFN = KT + (G - 1) * STEP_GROUP + HG
            PIECES = KT + CB

            def inverse_root(rs, means, i, stat, done):
                pool.wait_ge(stat, i + 1)
                nc.gpsimd.tensor_tensor(rs[:, i:i + 1], means[:, i, 1:2], half[:], ALU.pow).then_inc(done, 1)

            def split(parts, source, step, done):
                wait_apart()
                nc.gpsimd.tensor_scalar(parts[0], source, 1.0, 1.0, ALU.mult, ALU.mult).then_inc(pool_step, 1)
                pool.wait_ge(pool_step, step)
                nc.gpsimd.tensor_tensor(parts[1], source, parts[0].bitcast(F32), ALU.subtract).then_inc(done, 1)

            def wait_apart():
                pool.sem_inc(pool_passed, 1)

            def norm_head(g, i, h):
                pool.wait_ge(r_done, g * (NT * HG) + i * HG + h + 1)
                wait_apart()
                cols = (i + 1) * P
                nc.gpsimd.tensor_scalar(probs[:, h, 0:cols], probs[:, h, 0:cols], rsum[:, h:h + 1], 1.0,
                                        ALU.mult, ALU.mult).then_inc(p_ready, 1)

            def split_dense(g):
                pool.wait_ge(wd_in, 16 * g + 16)
                pool.wait_ge(y_done, g * NT + 1)
                for h in range(HG):
                    split([t[:, h, :] for t in wd], raw_wd[:, h, :], KT + g * STEP_GROUP + h + 1, wd_ready)
                pool.wait_ge(wd_ready, g * HG + HG)
                pool.sem_inc(raw_free, 1)

            def split_next(g, k):
                if k == 0:
                    pool.wait_ge(w_in, 16 * g + 32)
                    pool.wait_ge(t_full, T_PRO + g * T_GROUP + T_P[0])
                split([t[:, k, :] for t in w], raw_w[:, k, :], KT + g * STEP_GROUP + HG + k + 1, w_ready)
                if k == KT - 1:
                    pool.wait_ge(w_ready, KT * g + 2 * KT)
                    pool.sem_inc(raw_free, 1)

            def prepare(c, slot, k):
                if k < KT:
                    source, parts = raw_up[:, k, :], [t[:, k, 0:2 * CW] for t in (w, qT)[slot]]
                    table, at, n, done = s_up_b, c * (KT * 2 * CB) + k * 2 * CB, 2 * CB, up_ready
                else:
                    source, parts = raw_down[:, k - KT, :], [t[:, slot * CB + k - KT, :] for t in wd]
                    table, at, n, done = s_down_b, c * (CB * D // P) + (k - KT) * (D // P), D // P, down_ready
                blocks = source.rearrange("p (n c) -> p n c", c=P)
                scales = table[:, bass.ds(at, n)].unsqueeze(2).broadcast_to([P, n, P])
                step = STEP_FFN + c * (2 * PIECES) + 2 * k
                nc.gpsimd.tensor_tensor(blocks, blocks, scales, ALU.mult).then_inc(pool_step, 1)
                pool.wait_ge(pool_step, step + 1)
                split(parts, source, step + 2, done)
                if k == PIECES - 1:
                    pool.wait_ge(up_ready, c * KT + KT)
                    pool.wait_ge(down_ready, c * CB + CB)
                    pool.sem_inc(raw_free, 1)

            def quantise(tile, scale, inverse, done):
                wait_apart()
                for b in range(tile.shape[1] // P):
                    last = nc.gpsimd.tensor_scalar(tile[:, b * P:(b + 1) * P], tile[:, b * P:(b + 1) * P],
                                                   inverse[:, b:b + 1], scale[:, b:b + 1], ALU.mult, ALU.mult)
                last.then_inc(done, 1)

            def quantise_hidden(n, slot):
                pool.wait_ge(h_scaled, n + 1)
                quantise(h_sb[:, slot, :], hs[:, slot, :], hr[:, slot, :], h_ready)

            def feed_forward_chunk(c, slot, following):
                for i in range(NT):
                    quantise_hidden(c * NT + i, i % 2)
                    if not following:
                        continue
                    if i == 0:
                        pool.wait_ge(ffn_in, 32 * c + 64)
                        pool.wait_ge(gu_full, c * NT)
                    if i == KT:
                        pool.wait_ge(d_full, c * NT)
                    if i < PIECES:
                        prepare(c + 1, 1 - slot, i)

            nc.gpsimd.memset(half[:], -0.5).then_inc(const_ready, 1)
            nc.gpsimd.memset(ident[:], 0.0).then_inc(const_ready, 1)
            nc.gpsimd.memset(mask[:], 0.0).then_inc(const_ready, 1)
            pool.wait_ge(const_ready, 3)
            nc.gpsimd.affine_select(out=ident[:], in_=ident[:], compare_op=ALU.not_equal, fill=1.0, base=0,
                                    pattern=[[-1, P]], channel_multiplier=1).then_inc(const_ready, 1)
            nc.gpsimd.affine_select(out=mask[:, S - P:S], in_=mask[:, S - P:S], compare_op=ALU.is_ge, fill=NEG,
                                    base=0, pattern=[[-1, P]], channel_multiplier=1).then_inc(const_ready, 1)
            nc.gpsimd.memset(y[:], 0.0).then_inc(const_ready, 1)
            for i in range(NT):
                inverse_root(rstd, mv, i, stat_x, rstd_x)
                if i < KT:
                    if i == 0:
                        pool.wait_ge(w_in, 16)
                    split([t[:, i, :] for t in w], raw_w[:, i, :], i + 1, w_ready)
            pool.wait_ge(w_ready, KT)
            pool.sem_inc(raw_free, 1)

            with pool.Fori(0, G - 1) as g:
                split_dense(g)
                for i in range(NT):
                    for h in range(HG):
                        norm_head(g, i, h)
                    if NT - 1 - KT <= i < NT - 1:
                        split_next(g, i - (NT - 1 - KT))
            split_dense(G - 1)
            for i in range(NT):
                for h in range(HG):
                    norm_head(G - 1, i, h)
                if i == 0:
                    pool.wait_ge(scales_in, 32)
                    pool.wait_ge(ffn_in, 32)
                    pool.wait_ge(t_full, T_PRO + (G - 1) * T_GROUP + T_P[0])
                if NT - 1 - KT <= i < NT - 1:
                    prepare(0, 0, i - (NT - 1 - KT))
            for i in range(NT + 4):
                if i < NT:
                    inverse_root(rstd, mv, i, stat_y, rstd_y)
                if i == 0:
                    pool.wait_ge(y_full, G * NT)
                    for k in range(KT, PIECES):
                        prepare(0, 0, k)
                if 1 <= i <= NT:
                    inverse_root(rstd1, mv1, i - 1, stat_x1, rstd_x1)
                if 2 <= i <= NT + 1:
                    pool.wait_ge(scaled, i - 1)
                    quantise(y[:, i - 2, :], qs[:, i % 2, :], qr[:, i % 2, :], xn1_ready)
                if i >= 4:
                    n = i - 4
                    quantise_hidden(n, n % 2)
                    if n == 0:
                        pool.wait_ge(ffn_in, 64)
                    if n < PIECES:
                        prepare(1, 1, n)
            with pool.Fori(0, (C - 3) // 2) as r:
                for e in range(2):
                    feed_forward_chunk(2 * r + 1 + e, (1 + e) % 2, True)
            feed_forward_chunk(C - 2, 1, True)
            feed_forward_chunk(C - 1, 0, False)
            for i in range(NT + 1):
                if i < NT:
                    inverse_root(rstd, mv, i, stat_fin, rstd_fin)
                if i >= 1:
                    pool.wait_ge(z_ready, i)
                    nc.gpsimd.tensor_tensor(xt[:, i - 1, :], xt[:, i - 1, :], y[:, i - 1, :],
                                            ALU.add).then_inc(fin_ready, 1)

        @block.scalar
        def _(act):
            def hi_of_turn(dst, g, k):
                act.wait_ge(t_full, g * T_GROUP + T_PRO + k + 1)
                src = psT[:, k % 2, :]
                if dst.shape[1:] != src.shape[1:]:
                    src = psT[:, k % 2, 0:dst.shape[1] * P].rearrange("p (a b) -> p a b", b=P)
                nc.scalar.copy(dst, src).then_inc(t_hi, 1)

            def exponentials(g, i, h):
                act.wait_ge(s_done, g * (NT * HG) + 2 + i * HG + h + 1)
                row = probs[:, h, 0:(i + 1) * P]
                nc.scalar.activation(row, row, ACT.Exp, bias=negmax[:, h:h + 1], scale=-1.0,
                                     accum_out=lsum[:, h:h + 1]).then_inc(e_done, 1)

            def hi_of_xn(i, count):
                act.wait_ge(t_full, count)
                nc.scalar.copy(xnT[0][:, :, i * P:(i + 1) * P],
                               psT[:, i % 2, :].rearrange("p (a b) -> p a b", b=P)).then_inc(t_hi, 1)

            def silu_gate(n, slot):
                act.wait_ge(gu_full, n + 1)
                nc.scalar.activation(g_sb[:, slot, :], psS[:, slot, 0:CW], ACT.Silu).then_inc(g_done, 1)

            def hi_of_hidden(n, slot):
                act.wait_ge(ht_full, n + 1)
                nc.scalar.copy(pT[0][:, slot, 0:CW], psS[:, slot, BANK:BANK + CW]).then_inc(ht_hi, 1)

            for i in range(NT):
                hi_of_xn(i, i + 1)
            with act.Fori(0, G) as g:
                hi_of_turn(kT[0][:, 0:BANK], g, T_K[0])
                for h in range(HG):
                    hi_of_turn(qT[0][:, h, 0:BANK], g, T_Q[0] + h)
                hi_of_turn(kT[0][:, BANK:S], g, T_K[1])
                for b in range(NH):
                    hi_of_turn(v[0][:, b * TPB:(b + 1) * TPB, :], g, T_V + b)
                for h in range(HG):
                    exponentials(g, 0, h)
                for h in range(HG):
                    hi_of_turn(qT[0][:, h, BANK:S], g, T_Q[1] + h)
                for i in range(NT):
                    for h in range(HG):
                        for b in range(p_banks(i)):
                            hi_of_turn(pT[0][:, b * TPB:min((b + 1) * TPB, i + 1), h * P:(h + 1) * P], g, p_use(i, h, b))
                        if i < NT - 1 and h >= 1:
                            exponentials(g, i + 1, h - 1)
                    if i < NT - 1:
                        exponentials(g, i + 1, HG - 1)
                    act.wait_ge(o_full, g * NT + i + 1)
                    nc.scalar.copy(oT[0][:], psO).then_inc(o_hi, 1)
            for i in range(NT + 1):
                if i >= 1:
                    silu_gate(i - 1, (i - 1) % 2)
                if i < NT:
                    hi_of_xn(i, T_ATT + i + 1)
                if i >= 2:
                    hi_of_hidden(i - 2, i % 2)
            with act.Fori(0, (C - 1) // 2) as r:
                for m in range(2 * NT):
                    n = (2 * NT) * r + NT + m
                    silu_gate(n, m % 2)
                    hi_of_hidden(n - 1, (m - 1) % 2)
            hi_of_hidden(C * NT - 1, (C * NT - 1) % 2)

        @block.vector
        def _(dve):
            own = [0]

            def link(instruction):
                own[0] += 1
                instruction.then_inc(own_step, 1)
                dve.wait_ge(own_step, own[0])

            def lo_part(dst, psum, hi):
                return nc.vector.tensor_tensor(dst, psum, hi.bitcast(F32), ALU.subtract)

            def lo_of_turn(parts, g, k):
                dst = parts[1]
                dve.wait_ge(t_hi, g * H_GROUP + T_PRO + hi_count(k))
                src = psT[:, k % 2, :]
                if dst.shape[1:] != src.shape[1:]:
                    src = psT[:, k % 2, 0:dst.shape[1] * P].rearrange("p (a b) -> p a b", b=P)
                lo_part(dst, src, parts[0]).then_inc(t_done, 1)

            def copy_vt(g, half):
                dve.wait_ge(t_full, g * T_GROUP + T_PRO + T_VT[half] + 1)
                nc.vector.tensor_copy(probs[:, 0, half * BANK:(half + 1) * BANK],
                                      psT[:, T_VT[half] % 2, :]).then_inc(t_done, 1)

            def masked_max(g, i, h):
                dve.wait_ge(s_full, g * (NT * HG) + i * HG + h + 1)
                dve.sem_inc(dve_passed, 1)
                cols = (i + 1) * P
                nc.vector.tensor_tensor_reduce(out=probs[:, h, 0:cols], in0=psS[:, h % 2, 0:cols],
                                               in1=mask[:, S - cols:S], scale=-SCALE, scalar=-NEG,
                                               op0=ALU.add, op1=ALU.min,
                                               accum_out=negmax[:, h:h + 1]).then_inc(s_done, 1)

            def invert_sum(g, i, h):
                dve.wait_ge(e_done, g * (NT * HG) + i * HG + h + 1)
                nc.vector.reciprocal(rsum[:, h:h + 1], lsum[:, h:h + 1]).then_inc(r_done, 1)

            def add_projection(g, i):
                dve.wait_ge(y_full, g * NT + i + 1)
                nc.vector.tensor_tensor(y[:, i, :], psY, y[:, i, :], ALU.add).then_inc(y_done, 1)

            def statistics(src, i, means, done):
                link(nc.vector.bn_stats(st[:, i, :], src))
                link(nc.vector.bn_aggr(means[:, i, :], st[:, i, :]))
                nc.vector.tensor_scalar(means[:, i, 1:2], means[:, i, 1:2], EPS, None, ALU.add).then_inc(done, 1)

            def normalise(dst, src, means, rs, i):
                return nc.vector.tensor_scalar(dst, src, means[:, i, 0:1], rs[:, i:i + 1], ALU.subtract, ALU.mult)

            def lo_of_xn(i, count):
                dve.wait_ge(t_hi, count)
                cols = slice(i * P, (i + 1) * P)
                lo_part(xnT[1][:, :, cols], psT[:, i % 2, :].rearrange("p (a b) -> p a b", b=P),
                        xnT[0][:, :, cols]).then_inc(t_done, 1)

            def block_max(src, mx):
                return nc.vector.tensor_reduce(mx, src.rearrange("p (n c) -> p n c", c=P), AXX, ALU.max,
                                               apply_absolute_value=True)

            def block_scale(scale, mx):
                return nc.vector.tensor_scalar(scale, mx, 1.0 / FP8_MAX, SCALE_FLOOR, ALU.mult, ALU.add)

            def make_hidden(n, slot):
                dve.wait_ge(g_done, n + 1)
                nc.vector.tensor_tensor(h_sb[:, slot, :], psS[:, slot, CW:2 * CW], g_sb[:, slot, :],
                                        ALU.mult).then_inc(h_made, 1)
                dve.wait_ge(h_made, n + 1)
                block_max(h_sb[:, slot, :], hmax[:, slot, :]).then_inc(h_step, 1)
                dve.wait_ge(h_step, 2 * n + 1)
                block_scale(hs[:, slot, :], hmax[:, slot, :]).then_inc(h_step, 1)
                dve.wait_ge(h_step, 2 * n + 2)
                nc.vector.reciprocal(hr[:, slot, :], hs[:, slot, :]).then_inc(h_scaled, 1)

            def lo_of_hidden(n, slot):
                dve.wait_ge(ht_hi, n + 1)
                lo_part(pT[1][:, slot, 0:CW], psS[:, slot, BANK:BANK + CW], pT[0][:, slot, 0:CW]).then_inc(ht_done, 1)

            def add_down(n, i, first):
                dve.wait_ge(d_full, n + 1)
                if first:
                    nc.vector.tensor_copy(y[:, i, :], psOY[:, i % 2, :]).then_inc(d_done, 1)
                else:
                    nc.vector.tensor_tensor(y[:, i, :], psOY[:, i % 2, :], y[:, i, :], ALU.add).then_inc(d_done, 1)

            dve.sem_inc(s_done, 2)
            dve.sem_inc(o_done, 1)
            dve.sem_inc(y_done, 1)
            for i in range(NT + 2):
                if i < NT:
                    dve.wait_ge(x_in[i], 16)
                    statistics(xt[:, i, :], i, mv, stat_x)
                if 1 <= i <= NT:
                    dve.wait_ge(rstd_x, i)
                    normalise(xt[:, i - 1, :], xt[:, i - 1, :], mv, rstd, i - 1).then_inc(xn_ready, 1)
                if i >= 2:
                    lo_of_xn(i - 2, i - 1)
            dve.wait_ge(const_ready, 6)
            with dve.Fori(0, G) as g:
                lo_of_turn([t[:, 0:BANK] for t in kT], g, T_K[0])
                copy_vt(g, 0)
                for h in range(HG):
                    lo_of_turn([t[:, h, 0:BANK] for t in qT], g, T_Q[0] + h)
                lo_of_turn([t[:, BANK:S] for t in kT], g, T_K[1])
                copy_vt(g, 1)
                for b in range(NH):
                    lo_of_turn([t[:, b * TPB:(b + 1) * TPB, :] for t in v], g, T_V + b)
                for h in range(HG):
                    masked_max(g, 0, h)
                for h in range(HG):
                    invert_sum(g, 0, h)
                    lo_of_turn([t[:, h, BANK:S] for t in qT], g, T_Q[1] + h)
                for i in range(NT):
                    for h in range(HG):
                        for b in range(p_banks(i)):
                            lo_of_turn([t[:, b * TPB:min((b + 1) * TPB, i + 1), h * P:(h + 1) * P] for t in pT],
                                       g, p_use(i, h, b))
                        if i < NT - 1:
                            masked_max(g, i + 1, h)
                            if h >= 1:
                                invert_sum(g, i + 1, h - 1)
                    if i < NT - 1:
                        invert_sum(g, i + 1, HG - 1)
                    if i >= 1:
                        add_projection(g, i - 1)
                    dve.wait_ge(o_hi, g * NT + i + 1)
                    lo_part(oT[1][:], psO, oT[0][:]).then_inc(o_done, 1)
                add_projection(g, NT - 1)
            for i in range(NT + 4):
                if i < NT:
                    if i == 0:
                        dve.wait_ge(y_done, G * NT + 1)
                    statistics(y[:, i, :], i, mv, stat_y)
                if 1 <= i <= NT:
                    j = i - 1
                    dve.wait_ge(rstd_y, j + 1)
                    link(normalise(y[:, j, :], y[:, j, :], mv, rstd, j))
                    dve.wait_ge(x_in[j], 32)
                    link(nc.vector.tensor_tensor(xt[:, j, :], xt[:, j, :], y[:, j, :], ALU.add))
                    statistics(xt[:, j, :], j, mv1, stat_x1)
                if 2 <= i <= NT + 1:
                    j = i - 2
                    dve.wait_ge(rstd_x1, j + 1)
                    link(normalise(y[:, j, :], xt[:, j, :], mv1, rstd1, j))
                    link(block_max(y[:, j, :], amax[:, j % 2, :]))
                    link(block_scale(qs[:, j % 2, :], amax[:, j % 2, :]))
                    nc.vector.reciprocal(qr[:, j % 2, :], qs[:, j % 2, :]).then_inc(scaled, 1)
                if 3 <= i <= NT + 2:
                    j = i - 3
                    lo_of_xn(j, T_PRO + G * H_GROUP + j + 1)
                    if j >= NT - 2:
                        link(nc.vector.memset(y[:, j, :], 0.0))
                if i >= 4:
                    make_hidden(i - 4, i % 2)
                if i >= 5:
                    lo_of_hidden(i - 5, (i - 5) % 2)
                if i >= 6:
                    add_down(i - 6, i - 6, True)
            def feed_forward_step(n, m):
                make_hidden(n, m % 2)
                lo_of_hidden(n - 1, (m - 1) % 2)
                add_down(n - 2, (m - 2) % NT, False)

            with dve.Fori(0, (C - 1) // 2) as r:
                for m in range(2 * NT):
                    feed_forward_step((2 * NT) * r + NT + m, m)
            lo_of_hidden(C * NT - 1, 1)
            add_down(C * NT - 2, NT - 2, False)
            add_down(C * NT - 1, NT - 1, False)
            for i in range(NT + 1):
                if i < NT:
                    if i == 0:
                        dve.wait_ge(d_done, C * NT)
                    statistics(y[:, i, :], i, mv, stat_fin)
                if i >= 1:
                    dve.wait_ge(rstd_fin, i)
                    normalise(y[:, i - 1, :], y[:, i - 1, :], mv, rstd, i - 1).then_inc(z_ready, 1)

        @block.tensor
        def _(pe):
            def product(dst, pieces, **flags):
                terms = [t for lhs, rhs in pieces for t in split_passes(lhs, rhs)]
                for k, (a, b) in enumerate(terms):
                    last = nc.tensor.matmul(dst, a, b, start=(k == 0), stop=(k == len(terms) - 1))
                return last

            def turn_ring(g, k):
                pe.wait_ge(t_done, g * T_GROUP + T_PRO + k - 1)
                return psT[:, k % 2, :]

            def project(g, k, col, half):
                bank = turn_ring(g, k)
                product(bank, [([t[:, m, col:col + P] for t in w],
                                [t[:, m, half * BANK:(half + 1) * BANK] for t in xnT])
                               for m in range(KT)]).then_inc(t_full, 1)

            def turn_tile(src, i, ready, count, uses):
                pe.wait_ge(ready, count)
                if uses + i >= 2:
                    pe.wait_ge(t_done, uses + i - 1)
                for m in range(KT):
                    last = nc.tensor.transpose(psT[:, i % 2, m * P:(m + 1) * P], src[:, m * P:(m + 1) * P], ident[:])
                last.then_inc(t_full, 1)

            def turn_values(g, b):
                pe.wait_ge(t_done, g * T_GROUP + T_PRO + T_VT[b] + 1)
                bank = turn_ring(g, T_V + b)
                for m in range(TPB):
                    at = (b * TPB + m) * P
                    last = nc.tensor.transpose(bank[:, m * P:(m + 1) * P], probs[:, 0, at:at + P], ident[:])
                last.then_inc(t_full, 1)

            def scores(g, i, h):
                if i == 0 and h == 0:
                    pe.wait_ge(t_done, g * T_GROUP + T_PRO + T_V)
                if i == TPB and h == 0:
                    pe.wait_ge(t_done, g * T_GROUP + T_PRO + T_P[0])
                pe.wait_ge(s_done, g * (NT * HG) + i * HG + h + 1)
                for c in range(0, (i + 1) * P, BANK):
                    cols = max(2 * P, min(BANK, (i + 1) * P - c))
                    last = product(psS[:, h % 2, c:c + cols],
                                   [([t[:, h, i * P:(i + 1) * P] for t in qT], [t[:, c:c + cols] for t in kT])])
                last.then_inc(s_full, 1)

            def turn_probs(g, i, h):
                pe.wait_ge(p_ready, g * (NT * HG) + i * HG + h + 1)
                for b in range(p_banks(i)):
                    bank = turn_ring(g, p_use(i, h, b))
                    for j in range(b * TPB, min((b + 1) * TPB, i + 1)):
                        last = nc.tensor.transpose(bank[:, (j % TPB) * P:(j % TPB + 1) * P],
                                                   probs[:, h, j * P:(j + 1) * P], ident[:])
                    last.then_inc(t_full, 1)

            def weighted_values(g, i):
                pe.wait_ge(o_done, g * NT + i + 1)
                pe.wait_ge(t_done, g * T_GROUP + T_PRO + T_P[i + 1])
                product(psO, [([t[:, j, :] for t in v], [t[:, j, :] for t in pT])
                              for j in range(i + 1)]).then_inc(o_full, 1)

            def output_share(g, i, h):
                if h == 0:
                    pe.wait_ge(o_done, g * NT + i + 2)
                    pe.wait_ge(y_done, g * NT + i + 1)
                    if i == 0:
                        pe.wait_ge(wd_ready, g * HG + HG)
                terms = split_passes([t[:, h * P:(h + 1) * P] for t in oT], [t[:, h, :] for t in wd])
                for k, (a, b) in enumerate(terms):
                    last = nc.tensor.matmul(psY, a, b, start=(h == 0 and k == 0), stop=(h == HG - 1 and k == 2))
                if h == HG - 1:
                    last.then_inc(y_full, 1)

            def gate_up(n, slot, i, up):
                if not isinstance(n, int) or n >= 2:
                    pe.wait_ge(h_made, n - 1)
                product(psS[:, slot, 0:BANK], [([t[:, m, i * P:(i + 1) * P] for t in xnT], [t[:, m, :] for t in up])
                                               for m in range(KT)]).then_inc(gu_full, 1)

            def turn_hidden(n, slot):
                pe.wait_ge(h_ready, n + 1)
                if not isinstance(n, int) or n >= 2:
                    pe.wait_ge(ht_done, n - 1)
                for m in range(CB):
                    last = nc.tensor.transpose(psS[:, slot, BANK + m * P:BANK + (m + 1) * P],
                                               h_sb[:, slot, m * P:(m + 1) * P], ident[:])
                last.then_inc(ht_full, 1)

            def down(n, slot, weights):
                pe.wait_ge(ht_done, n + 1)
                if not isinstance(n, int) or n >= 2:
                    pe.wait_ge(d_done, n - 1)
                product(psOY[:, slot, :], [([t[:, slot, m * P:(m + 1) * P] for t in pT],
                                            [t[:, weights * CB + m, :] for t in wd])
                                           for m in range(CB)]).then_inc(d_full, 1)

            up_place = [[t[:, :, 0:2 * CW] for t in w], [t[:, :, 0:2 * CW] for t in qT]]

            pe.wait_ge(const_ready, 4)
            for i in range(NT):
                turn_tile(xt[:, i, :], i, xn_ready, i + 1, 0)
            with pe.Fori(0, G) as g:
                pe.wait_ge(w_ready, KT * g + KT)
                pe.wait_ge(t_done, NT // 2)
                project(g, T_K[0], K_COL, 0)
                project(g, T_VT[0], V_COL, 0)
                for h in range(HG):
                    project(g, T_Q[0] + h, h * P, 0)
                pe.wait_ge(t_done, NT)
                project(g, T_K[1], K_COL, 1)
                project(g, T_VT[1], V_COL, 1)
                turn_values(g, 0)
                turn_values(g, 1)
                for h in range(HG):
                    scores(g, 0, h)
                for h in range(HG):
                    project(g, T_Q[1] + h, h * P, 1)
                for i in range(NT):
                    for h in range(HG):
                        turn_probs(g, i, h)
                        if i < NT - 1:
                            scores(g, i + 1, h)
                        if i >= 1:
                            output_share(g, i - 1, h)
                    weighted_values(g, i)
                for h in range(HG):
                    output_share(g, NT - 1, h)
            for i in range(NT + 1):
                if i >= 1:
                    if i == 1:
                        pe.wait_ge(up_ready, KT)
                        pe.wait_ge(s_done, G * NT * HG + 2)
                    pe.wait_ge(t_done, T_ATT + i)
                    gate_up(i - 1, (i - 1) % 2, i - 1, up_place[0])
                if i < NT:
                    turn_tile(y[:, i, :], i, xn1_ready, i + 1, T_ATT)
                if i >= 3:
                    if i == 3:
                        pe.wait_ge(down_ready, CB)
                        pe.wait_ge(y_done, G * NT + 1)
                    down(i - 3, (i - 3) % 2, 0)
                if i >= 2:
                    turn_hidden(i - 2, i % 2)
            with pe.Fori(0, (C - 1) // 2) as r:
                for m in range(2 * NT):
                    n = (2 * NT) * r + NT + m
                    parity = (m // NT + 1) % 2
                    if m % NT == 0:
                        pe.wait_ge(up_ready, (2 * KT) * r + (2 + m // NT) * KT)
                    gate_up(n, m % 2, m % NT, up_place[parity])
                    if m % NT == 2:
                        pe.wait_ge(down_ready, (2 * CB) * r + (2 + m // NT) * CB)
                    down(n - 2, m % 2, parity if m % NT >= 2 else 1 - parity)
                    turn_hidden(n - 1, (m - 1) % 2)
            down(C * NT - 2, 0, (C - 1) % 2)
            turn_hidden(C * NT - 1, 1)
            down(C * NT - 1, 1, (C - 1) % 2)


def kernel(L0_attn_q, L0_attn_w_qkv, L0_attn_w_dense, L0_ffn_w1, L0_ffn_w1_scale, L0_ffn_w3, L0_ffn_w3_scale,
           L0_ffn_w2, L0_ffn_w2_scale):
    import concourse.bacc as bacc
    import numpy as np
    from concourse.bass_utils import run_bass_kernel_spmd

    x = np.ascontiguousarray(L0_attn_q)[0]
    S, D = x.shape
    KT, G, HG, C = D // P, 8, 4, 7
    qkv, wd = np.ascontiguousarray(L0_attn_w_qkv), np.ascontiguousarray(L0_attn_w_dense)
    nq, nkv = G * HG * P, G * P
    rows = np.concatenate([qkv[:nq].reshape(G, HG * P, D), qkv[nq:nq + nkv].reshape(G, P, D),
                           qkv[nq + nkv:].reshape(G, P, D)], axis=1)
    w_attn = rows.reshape(G, (HG + 2) * P, KT, P).transpose(0, 3, 2, 1)
    w_dense = wd.reshape(D, G, HG, P).transpose(1, 3, 2, 0)
    w1, w3, w2 = (np.ascontiguousarray(a) for a in (L0_ffn_w1, L0_ffn_w3, L0_ffn_w2))
    F = w1.shape[0]
    CW = F // C
    CB = CW // P
    w_up = np.concatenate([a.reshape(C, CW, KT, P).transpose(0, 3, 2, 1) for a in (w1, w3)], axis=3)
    w_down = w2.reshape(D, C, CB, P).transpose(1, 3, 2, 0)
    s1, s3, s2 = (np.ascontiguousarray(a) for a in (L0_ffn_w1_scale, L0_ffn_w3_scale, L0_ffn_w2_scale))
    s_up = np.concatenate([a.reshape(C, CB, KT).transpose(0, 2, 1) for a in (s1, s3)], axis=2).reshape(1, -1)
    s_down = s2.reshape(D // P, C, CB).transpose(1, 2, 0).reshape(1, -1)

    nc = bacc.Bacc("TRN2", target_bir_lowering=False, num_devices=1)
    arrays, args = {}, []
    for name, a in (("x", x), ("w_attn", w_attn), ("w_dense", w_dense), ("w_up", w_up), ("w_down", w_down),
                    ("s_up", s_up), ("s_down", s_down)):
        arrays[f"in_{name}"] = np.ascontiguousarray(a)
        args.append(nc.dram_tensor(f"in_{name}", a.shape, F32, kind="ExternalInput").ap())
    args.append(nc.dram_tensor("result", (S, D), F32, kind="ExternalOutput").ap())
    sandwich_kernel(nc, *args)
    r = run_bass_kernel_spmd(nc, [arrays], core_ids=[0])
    return r.results[0]["result"].reshape(1, S, D)
```

```python
from contextlib import ExitStack

import concourse.bass as bass
from concourse import mybir

F32 = mybir.dt.float32
F32R = mybir.dt.float32r
ALU = mybir.AluOpType
ACT = mybir.ActivationFunctionType
AXX = mybir.AxisListType.X

P = 128
BANK = 512
NEG = -1.0e38
EPS = 1e-5
FP8_MAX = 448.0
SCALE_FLOOR = 1e-12


def sandwich_kernel(nc, x, w_attn, w_dense, w_up, w_down, s_up, s_down, out):
    S, D = x.shape
    G = w_attn.shape[0]
    KT = D // P
    WC = w_attn.shape[3]
    HG = WC // P - 2
    NT = S // P
    NH = S // BANK
    C = w_up.shape[0]
    CW = w_up.shape[3] // 2
    CB = CW // P
    SCALE = float(P) ** -0.5
    K_COL, V_COL = HG * P, (HG + 1) * P
    TPB = BANK // P
    assert D == BANK and HG == TPB and HG * P == D and C % 2 == 1 and 2 * CW == BANK and NH == 2

    ORDER = [t for a in range(NT // 2) for t in (a, NT - 1 - a)]

    def p_banks(s):
        return (ORDER[s] + TPB) // TPB

    NORMS = [[("center_y", 2), ("scales", 4)], [("norm_y", 2)], [("center_x1", 3), ("residual", 2)],
             [("norm_x1", 3), ("stat_x1", 2)]]

    def step_items(s, last):
        items, following, two = [], s < NT - 1, p_banks(s) == 2
        if not two:
            shares = [[], [0], [1], [2, 3]]
        else:
            shares = [[], [0], [1], []] if following else [[], [0, 1], [], [2]]
        exps = [("E", s, HG - 1)] if s == 1 else []
        exps += [("E", s + 1, h) for h in range(HG - 1 if s == 0 else HG) if following]
        for h in range(HG):
            items.append(("P", s, 0, h))
            if following:
                items.append(("S", s + 1, h))
            elif h == 0 and not last:
                items.append(("K", 0))
            if s == 1 or h >= 1:
                items += exps[:1]
                del exps[:1]
            if s >= 1:
                items += [("Y", s - 1, head) for head in shares[h]]
            if last:
                items += [(kind, s - lag) for kind, lag in NORMS[h] if s >= lag]
        if two:
            if following:
                items += [("P", s, 1, 0), *exps, ("Y", s - 1, 2), ("P", s, 1, 1), ("Y", s - 1, 3),
                          ("P", s, 1, 2), ("PV", s, 0), ("P", s, 1, 3), ("PV", s, 1)]
            else:
                items += [("P", s, 1, 0), ("Y", s - 1, 3), ("P", s, 1, 1), *([] if last else [("Q", 0, 0)]),
                          ("P", s, 1, 2), ("PV", s, 0), ("PV", s, 1), ("P", s, 1, 3)]
        items += exps if not two else []
        if s >= 1:
            items.append(("A", s - 1))
        if last:
            if 1 <= s <= KT or s >= NT - CB:
                items.append(("W", s - 1 if s <= KT else KT + s - (NT - CB)))
            items += [(kind, s - lag) for kind, lag in (("stat_y", 1), ("root_y", 1), ("root_x1", 2), ("quantise", 4))
                      if s >= lag]
        items += [("PV", s, j) for j in range(2 if two else 0, ORDER[s] + 1)]
        items.append(("O", s))
        if not last and 1 <= s <= KT:
            items.append(("W", s - 1))
        return items

    def ending(share):
        return [("K", 1), ("S", 0, 0), ("VT", 1), ("S", 0, 1), ("Q", 1, 0), ("V", 1), ("S", 0, 2), ("S", 0, 3), *share,
                ("E", 0, 0), ("E", 0, 1), ("Q", 1, 1), ("E", 0, 2), ("E", 0, 3), ("Q", 1, 2), ("Q", 1, 3)]

    PROLOGUE = [*(("X", i) for i in range(TPB)), ("K", 0), ("X", 4), ("VT", 0), ("X", 5), ("Q", 0, 0), ("X", 6),
                ("V", 0), ("X", 7), ("Q", 0, 1), ("Q", 0, 2), ("Q", 0, 3)] + ending([])
    GROUP = ([item for s in range(NT) for item in step_items(s, False)]
             + [("VT", 0), *(("Y", NT - 1, h) for h in range(HG - 1)), ("V", 0), ("Q", 0, 1), ("Q", 0, 2), ("Q", 0, 3)]
             + ending([("Y", NT - 1, HG - 1)]) + [("A", NT - 1), ("D",)])
    LAST_GROUP = [item for s in range(NT) for item in step_items(s, True)]

    def turns(items):
        return [item for item in items if item[0] in ("X", "K", "Q", "VT", "V", "P")]

    def copies(items):
        return [item for item in turns(items) if item[0] != "VT"]

    class Part:

        def __init__(self, items, g, uses, hi_copies):
            self.items, self.g, self.uses, self.hi_copies = items, g, uses, hi_copies
            self.first = items is PROLOGUE
            self.turn = {item: k for k, item in enumerate(turns(items))}
            self.copy = {item: k for k, item in enumerate(copies(items))}
            ring = [item for item in turns(items) if item[0] != "X"]
            self.bank = {item: k % 2 for k, item in enumerate(ring)}

        def place(self, item):
            if item[0] == "X":
                return psS[:, item[1] % 4 // 2, item[1] % 2 * BANK:(item[1] % 2 + 1) * BANK]
            return psT[:, self.bank[item], :]

        def before(self, item):
            same = [k for other, k in self.turn.items() if k < self.turn[item]
                    and (other[0] == item[0] == "X" and other[1] % 4 == item[1] % 4
                         or "X" not in (other[0], item[0]) and self.bank[other] == self.bank[item])]
            return max(same) + 1 if same else 0

        def use(self, item):
            return self.uses + self.turn[item]

        def hi(self, item):
            return self.hi_copies + self.copy[item] + 1

    T_PRO, T_GROUP = len(turns(PROLOGUE)), len(turns(GROUP))
    H_PRO, H_GROUP = len(copies(PROLOGUE)), len(copies(GROUP))
    T_LAST = T_PRO + (G - 1) * T_GROUP
    T_ATT = T_LAST + len(turns(LAST_GROUP))
    H_ATT = H_PRO + (G - 1) * H_GROUP + len(copies(LAST_GROUP))
    assert (T_PRO - NT) % 2 == 0 and T_GROUP % 2 == 0 and T_ATT % 2 == 0

    def prologue():
        return Part(PROLOGUE, -1, 0, 0)

    def group(g):
        return Part(GROUP, g, T_GROUP * g + T_PRO, H_GROUP * g + H_PRO)

    def last_group():
        return Part(LAST_GROUP, G - 1, T_LAST, H_PRO + (G - 1) * H_GROUP)

    with ExitStack() as ctx:
        def sb(name, shape, dt=F32):
            return ctx.enter_context(nc.sbuf_tensor(name, shape, dt))

        def sem(name):
            return ctx.enter_context(nc.semaphore(name))

        xnT_hi = sb("xnT_hi", [P, KT, S], F32R)
        xnT_lo_at = nc.sbuf_base
        xnT = [xnT_hi, sb("xnT_lo", [P, KT, S], F32R)]
        w = [sb(f"w_{p}", [P, KT, WC], F32R) for p in ("hi", "lo")]
        qT = [sb(f"qT_{p}", [P, HG, S], F32R) for p in ("hi", "lo")]
        kT = [sb(f"kT_{p}", [P, S], F32R) for p in ("hi", "lo")]
        v = [sb(f"v_{p}", [P, NT, P], F32R) for p in ("hi", "lo")]
        wd = [sb(f"wd_{p}", [P, HG, D], F32R) for p in ("hi", "lo")]
        pT = [sb(f"pT_{p}", [P, NT, BANK], F32R) for p in ("hi", "lo")]
        oT = [sb(f"oT_{p}", [P, BANK], F32R) for p in ("hi", "lo")]
        probs = sb("probs", [P, HG, S])
        vt = sb("vt", [P, BANK])
        xt = probs[:].rearrange("p h (u d) -> p (h u) d", d=D)
        y = sb("y", [P, NT, D])
        raw = sb("raw", [P, KT * WC])
        mask = sb("mask", [P, S])
        ident = sb("ident", [P, P])
        s_up_b = sb("s_up_b", [P, s_up.shape[1]])
        s_down_b = sb("s_down_b", [P, s_down.shape[1]])
        negmax = sb("negmax", [P, HG])
        lsum = sb("lsum", [P, HG])
        rsum = sb("rsum", [P, HG])
        st = sb("st", [P, 2, 6])
        mv = sb("mv", [P, NT, 2])
        mv1 = sb("mv1", [P, NT, 2])
        rstd = sb("rstd", [P, NT])
        rstd1 = sb("rstd1", [P, NT])
        nmean = sb("nmean", [P, NT])
        nmean1 = sb("nmean1", [P, NT])
        half = sb("half", [P, 1])
        amax = sb("amax", [P, 2, KT])
        qs = sb("qs", [P, 2, KT])
        qr = sb("qr", [P, 2, KT])
        hmax = sb("hmax", [P, 2, CB])
        hs = sb("hs", [P, 2, CB])
        hr = sb("hr", [P, 2, CB])
        x1 = nc.alloc_sbuf_tensor_at("x1", [P, NT, D], F32, offset=xnT_lo_at)
        xn1T = [xnT_hi[:], pT[1][:].rearrange("p j c -> p (j c)").rearrange("p (k s) -> p k s", k=KT)]
        hT = [t[:].rearrange("p (s c) -> p s c", c=CW) for t in kT]
        g_sb = mask[:, 0:2 * CW].rearrange("p (s c) -> p s c", s=2)
        h_sb = mask[:, 2 * CW:4 * CW].rearrange("p (s c) -> p s c", s=2)

        raw_w = raw[:].rearrange("p (k c) -> p k c", k=KT)
        raw_wd = raw[:, 0:HG * D].rearrange("p (h d) -> p h d", h=HG)
        down_w = [t[:, :, 2 * CW:2 * CW + D] for t in qT]
        UPC = KT * 2 * CW
        raw_up = raw[:, 0:UPC].rearrange("p (k c) -> p k c", k=KT)
        raw_down = raw[:, UPC:UPC + CB * D].rearrange("p (k d) -> p k d", k=CB)

        psS = ctx.enter_context(nc.psum_tensor("psS", [P, 2, S], F32))
        psT = ctx.enter_context(nc.psum_tensor("psT", [P, 2, BANK], F32))
        psOY = ctx.enter_context(nc.psum_tensor("psOY", [P, 2, BANK], F32))
        psO, psY = psOY[:, 0, :], psOY[:, 1, :]

        x_in = [sem(f"x_in{i}") for i in range(NT)]
        scales_in = sem("scales_in")
        w0_in = [sem(f"w0_in{k}") for k in range(KT)]
        w0_hi = sem("w0_hi")
        w_in = sem("w_in")
        wd_in = sem("wd_in")
        ffn_in = sem("ffn_in")
        out_done = sem("out_done")
        raw_free = sem("raw_free")
        const_ready = sem("const_ready")
        pool_passed = sem("pool_passed")
        dve_passed = sem("dve_passed")
        pool_step = sem("pool_step")
        w_ready = sem("w_ready")
        wd_ready = sem("wd_ready")
        stat_x, stat_y, stat_x1, stat_fin = (sem(f"stat_{n}") for n in ("x", "y", "x1", "fin"))
        rstd_x = sem("rstd_x")
        rstd_fin = sem("rstd_fin")
        rstd_y, rstd_x1 = sem("rstd_y"), sem("rstd_x1")
        centered = sem("centered")
        yn_ready = sem("yn_ready")
        x1n_ready = sem("x1n_ready")
        own_step = sem("own_step")
        xn_ready = sem("xn_ready")
        xn1_ready = sem("xn1_ready")
        t_full = sem("t_full")
        t_hi = sem("t_hi")
        t_done = sem("t_done")
        s_full = sem("s_full")
        s_done = sem("s_done")
        e_done = sem("e_done")
        r_done = sem("r_done")
        p_ready = sem("p_ready")
        o_full = sem("o_full")
        o_hi = sem("o_hi")
        o_done = sem("o_done")
        y_full = sem("y_full")
        y_done = sem("y_done")
        scaled = sem("scaled")
        up_ready = sem("up_ready")
        down_ready = sem("down_ready")
        gu_full = sem("gu_full")
        g_done = sem("g_done")
        h_made = sem("h_made")
        h_step = sem("h_step")
        h_scaled = sem("h_scaled")
        h_ready = sem("h_ready")
        ht_full = sem("ht_full")
        ht_hi = sem("ht_hi")
        ht_done = sem("ht_done")
        d_full = sem("d_full")
        d_done = sem("d_done")
        z_ready = sem("z_ready")
        fin_ready = sem("fin_ready")
        last_ready = sem("last_ready")

        block = ctx.enter_context(nc.Block())

        def score_offset(i):
            return P if (i + 1) * P > BANK and (i + 1) * P % BANK == P else 0

        def softmax_count(part, s, h):
            return (part.g + (1 if s == 0 else 0)) * (NT * HG) + s * HG + h + 1

        def behind(item):
            back = {len(turns(p)) - 1 - turns(p).index(item) for p in (PROLOGUE, GROUP)}
            assert len(back) == 1
            return back.pop()

        def tile_of(t, i):
            return t[:, :, i * P:(i + 1) * P]

        def free_size(ap):
            return ap.shape[1] * (ap.shape[2] if len(ap.shape) == 3 else 1)

        def turned(item):
            kind, *a = item
            if kind == "X":
                return [tile_of(t, a[0]) for t in xnT]
            if kind == "K":
                return [t[:, a[0] * BANK:(a[0] + 1) * BANK] for t in kT]
            if kind == "Q":
                return [t[:, a[1], a[0] * BANK:(a[0] + 1) * BANK] for t in qT]
            if kind == "V":
                return [t[:, a[0] * TPB:(a[0] + 1) * TPB, :] for t in v]
            s, b, h = a
            return [t[:, b * TPB:min((b + 1) * TPB, ORDER[s] + 1), h * P:(h + 1) * P] for t in pT]

        def split_passes(a, b):
            (a_hi, a_lo), (b_hi, b_lo) = a, b
            return [(a_hi, b_hi), (a_hi, b_lo), (a_lo, b_hi)]

        @block.sync
        def _(sp):
            for i in range(NT):
                sp.dma_start(xt[:, i, :], x[i * P:(i + 1) * P, :]).then_inc(x_in[i], 16)
                if i in (TPB - 2, TPB - 1):
                    for k in range(KT)[:1] if i == TPB - 2 else range(KT)[1:]:
                        sp.dma_start(raw_w[:, k, :], w_attn[0][:, k, :]).then_inc(w0_in[k], 16)
            for table, source in ((s_up_b, s_up), (s_down_b, s_down)):
                sp.dma_start(table[:], source.broadcast_to([P, source.shape[1]])).then_inc(scales_in, 16)
            sp.wait_ge(raw_free, 1)
            sp.dma_start(raw_wd, w_dense[0]).then_inc(wd_in, 16)
            with sp.Fori(0, G - 1) as g:
                sp.wait_ge(raw_free, 2 * g + 2)
                sp.dma_start(raw_w, w_attn[g + 1]).then_inc(w_in, 16)
                sp.wait_ge(raw_free, 2 * g + 3)
                sp.dma_start(raw_wd, w_dense[g + 1]).then_inc(wd_in, 16)
            sp.wait_ge(raw_free, 2 * G)
            sp.dma_start(raw_up, w_up[0]).then_inc(ffn_in, 16)
            sp.dma_start(raw_down, w_down[0]).then_inc(ffn_in, 16)
            sp.wait_ge(t_full, T_LAST)
            for i in ORDER:
                sp.dma_start(x1[:, i, :], x[i * P:(i + 1) * P, :]).then_inc(x_in[i], 16)
            with sp.Fori(1, C) as c:
                sp.wait_ge(raw_free, 2 * G + c)
                sp.dma_start(raw_up, w_up[c]).then_inc(ffn_in, 16)
                sp.dma_start(raw_down, w_down[c]).then_inc(ffn_in, 16)
            for s, i in enumerate(ORDER):
                if s < NT - 1:
                    sp.wait_ge(fin_ready, s + 1)
                else:
                    sp.wait_ge(last_ready, 1)
                sp.dma_start(out[i * P:(i + 1) * P, :], x1[:, i, :]).then_inc(out_done, 16)
            sp.wait_ge(out_done, 16 * NT)

        @block.gpsimd
        def _(pool):
            STEP_GROUP = HG + KT
            STEP_FFN = (G - 1) * STEP_GROUP + HG
            PIECES = KT + CB

            def inverse_root(rs, means, i, stat, done):
                pool.wait_ge(stat, i + 1)
                nc.gpsimd.tensor_tensor(rs[:, i:i + 1], means[:, i, 1:2], half[:], ALU.pow).then_inc(done, 1)

            def split(parts, source, step, done):
                wait_apart()
                nc.gpsimd.tensor_scalar(parts[0], source, 1.0, 1.0, ALU.mult, ALU.mult).then_inc(pool_step, 1)
                pool.wait_ge(pool_step, step)
                nc.gpsimd.tensor_tensor(parts[1], source, parts[0].bitcast(F32), ALU.subtract).then_inc(done, 1)

            def wait_apart():
                pool.sem_inc(pool_passed, 1)

            def norm_head(part, s, h):
                pool.wait_ge(r_done, softmax_count(part, s, h))
                wait_apart()
                cols = (ORDER[s] + 1) * P
                nc.gpsimd.tensor_scalar(probs[:, h, 0:cols], probs[:, h, 0:cols], rsum[:, h:h + 1], 1.0,
                                        ALU.mult, ALU.mult).then_inc(p_ready, 1)

            def w0_lo(k):
                pool.wait_ge(w0_hi, k + 1)
                nc.gpsimd.tensor_tensor(w[1][:, k, :], raw_w[:, k, :], w[0][:, k, :].bitcast(F32),
                                        ALU.subtract).then_inc(w_ready, 1)

            def split_projections(g, k):
                split([t[:, k, :] for t in w], raw_w[:, k, :], (g - 1) * STEP_GROUP + HG + k + 1, w_ready)
                if k == KT - 1:
                    pool.wait_ge(w_ready, g * KT + KT)
                    pool.sem_inc(raw_free, 1)

            def split_dense(g):
                pool.wait_ge(wd_in, 16 * g + 16)
                for h in range(HG):
                    split([t[:, h, :] for t in wd], raw_wd[:, h, :], g * STEP_GROUP + h + 1, wd_ready)
                pool.wait_ge(wd_ready, g * HG + HG)
                pool.sem_inc(raw_free, 1)

            def prepare(c, slot, k):
                if k < KT:
                    source, parts = raw_up[:, k, :], [t[:, k, 0:2 * CW] for t in (w, qT)[slot]]
                    table, at, n, done = s_up_b, c * (KT * 2 * CB) + k * 2 * CB, 2 * CB, up_ready
                else:
                    source, parts = raw_down[:, k - KT, :], [t[:, slot * CB + k - KT, :] for t in down_w]
                    table, at, n, done = s_down_b, c * (CB * D // P) + (k - KT) * (D // P), D // P, down_ready
                blocks = source.rearrange("p (n c) -> p n c", c=P)
                scales = table[:, bass.ds(at, n)].unsqueeze(2).broadcast_to([P, n, P])
                step = STEP_FFN + c * (2 * PIECES) + 2 * k
                nc.gpsimd.tensor_tensor(blocks, blocks, scales, ALU.mult).then_inc(pool_step, 1)
                pool.wait_ge(pool_step, step + 1)
                split(parts, source, step + 2, done)
                if k == PIECES - 1:
                    pool.wait_ge(up_ready, c * KT + KT)
                    pool.wait_ge(down_ready, c * CB + CB)
                    pool.sem_inc(raw_free, 1)

            def quantise(tile, scale, inverse, done):
                wait_apart()
                for b in range(tile.shape[1] // P):
                    last = nc.gpsimd.tensor_scalar(tile[:, b * P:(b + 1) * P], tile[:, b * P:(b + 1) * P],
                                                   inverse[:, b:b + 1], scale[:, b:b + 1], ALU.mult, ALU.mult)
                last.then_inc(done, 1)

            def quantise_hidden(n, slot):
                pool.wait_ge(h_scaled, n + 1)
                quantise(h_sb[:, slot, :], hs[:, slot, :], hr[:, slot, :], h_ready)

            def feed_forward_chunk(c, slot, following):
                for i in range(NT):
                    quantise_hidden(c * NT + i, i % 2)
                    if following:
                        if i == 0:
                            pool.wait_ge(ffn_in, 32 * c + 64)
                            pool.wait_ge(gu_full, c * NT)
                        if i == KT:
                            pool.wait_ge(d_full, c * NT)
                        if i < PIECES:
                            prepare(c + 1, 1 - slot, i)
                    elif i >= 2:
                        finish(i - 2)

            def finish(s):
                if s < NT:
                    inverse_root(rstd, mv, s, stat_fin, rstd_fin)
                if s >= 1:
                    i = ORDER[s - 1]
                    pool.wait_ge(z_ready, s)
                    nc.gpsimd.tensor_tensor(x1[:, i, :], x1[:, i, :], y[:, i, :], ALU.add).then_inc(fin_ready, 1)

            nc.gpsimd.memset(half[:], -0.5).then_inc(const_ready, 1)
            nc.gpsimd.memset(ident[:], 0.0).then_inc(const_ready, 1)
            nc.gpsimd.memset(mask[:], 0.0).then_inc(const_ready, 1)
            pool.wait_ge(const_ready, 3)
            nc.gpsimd.affine_select(out=ident[:], in_=ident[:], compare_op=ALU.not_equal, fill=1.0, base=0,
                                    pattern=[[-1, P]], channel_multiplier=1).then_inc(const_ready, 1)
            nc.gpsimd.affine_select(out=mask[:, S - P:S], in_=mask[:, S - P:S], compare_op=ALU.is_ge, fill=NEG,
                                    base=0, pattern=[[-1, P]], channel_multiplier=1).then_inc(const_ready, 1)
            for i in range(NT):
                inverse_root(rstd, mv, i, stat_x, rstd_x)
                if i == TPB - 2:
                    w0_lo(0)
                if i == TPB - 1:
                    for k in range(1, KT - 1):
                        w0_lo(k)
            pool.wait_ge(w_ready, KT)
            pool.sem_inc(raw_free, 1)
            nc.gpsimd.memset(y[:], 0.0).then_inc(const_ready, 1)
            split_dense(0)
            for h in range(HG):
                norm_head(prologue(), 0, h)

            with pool.Fori(0, G - 1) as g:
                part = group(g)
                for kind, *args in part.items:
                    if kind == "E":
                        norm_head(part, *args)
                    elif kind == "W":
                        if args == [0]:
                            pool.wait_ge(w_in, 16 * g + 16)
                            pool.wait_ge(t_full, part.uses)
                        split_projections(g + 1, *args)
                    elif kind == "D":
                        pool.wait_ge(y_full, g * NT + NT)
                        split_dense(g + 1)

            def root_y(s):
                inverse_root(rstd, mv, s, stat_y, rstd_y)

            def root_x1(s):
                inverse_root(rstd1, mv1, s, stat_x1, rstd_x1)

            def quantise_tile(s):
                pool.wait_ge(scaled, s + 1)
                quantise(y[:, ORDER[s], :], qs[:, s % 2, :], qr[:, s % 2, :], xn1_ready)

            part = last_group()
            for kind, *args in part.items:
                if kind == "E":
                    norm_head(part, *args)
                elif kind == "W":
                    if args == [0]:
                        pool.wait_ge(scales_in, 32)
                        pool.wait_ge(ffn_in, 32)
                        pool.wait_ge(t_full, T_LAST)
                    if args == [KT]:
                        pool.wait_ge(s_full, G * NT * HG)
                    prepare(0, 0, *args)
                elif kind == "root_y":
                    root_y(*args)
                elif kind == "root_x1":
                    root_x1(*args)
                elif kind == "quantise":
                    quantise_tile(*args)
            root_y(NT - 1)
            quantise_tile(NT - 4)
            root_x1(NT - 2)
            for n in range(NT):
                quantise_hidden(n, n % 2)
                if n < 3:
                    quantise_tile(NT - 3 + n)
                if n == 0:
                    root_x1(NT - 1)
                if n == 1:
                    pool.wait_ge(ffn_in, 64)
                if 1 <= n <= PIECES:
                    prepare(1, 1, n - 1)
            with pool.Fori(0, (C - 3) // 2) as r:
                for e in range(2):
                    feed_forward_chunk(2 * r + 1 + e, (1 + e) % 2, True)
            feed_forward_chunk(C - 2, 1, True)
            feed_forward_chunk(C - 1, 0, False)
            for s in (NT - 2, NT - 1):
                finish(s)

        @block.scalar
        def _(act):
            def hi_of_turn(dst, bank, count):
                act.wait_ge(t_full, count)
                src = bank[:, 0:free_size(dst)]
                if len(dst.shape) == 3:
                    src = src.rearrange("p (a b) -> p a b", b=P)
                nc.scalar.copy(dst, src).then_inc(t_hi, 1)

            def exponentials(part, s, h):
                act.wait_ge(s_done, 2 + softmax_count(part, s, h))
                row = probs[:, h, 0:(ORDER[s] + 1) * P]
                nc.scalar.activation(row, row, ACT.Exp, bias=negmax[:, h:h + 1], scale=-1.0,
                                     accum_out=lsum[:, h:h + 1]).then_inc(e_done, 1)

            def center(dst, src, negmean, s, stat):
                act.wait_ge(stat, s + 1)
                nc.scalar.activation(dst, src, ACT.Identity, bias=negmean[:, s:s + 1]).then_inc(centered, 1)

            def norm(dst, rs, s, root, uses, done):
                act.wait_ge(centered, uses)
                act.wait_ge(root, s + 1)
                nc.scalar.activation(dst, dst, ACT.Copy, scale=rs[:, s:s + 1]).then_inc(done, 1)

            def norms(kind, s):
                tile = y[:, ORDER[s], :]
                if kind == "center_y":
                    center(tile, tile, nmean, s, stat_y)
                elif kind == "norm_y":
                    norm(tile, rstd, s, rstd_y, max(2 * s, 1), yn_ready)
                elif kind == "center_x1":
                    center(tile, x1[:, ORDER[s], :], nmean1, s, stat_x1)
                elif kind == "norm_x1":
                    norm(tile, rstd1, s, rstd_x1, min(2 * s + 3, 2 * NT), x1n_ready)

            def attention(part):
                for item in part.items:
                    kind, *args = item
                    if item in part.copy:
                        hi_of_turn(turned(item)[0], part.place(item), part.use(item) + 1)
                        if kind == "X" and args[0] < KT:
                            act.wait_ge(w0_in[args[0]], 16)
                            nc.scalar.copy(w[0][:, args[0], :], raw_w[:, args[0], :]).then_inc(w0_hi, 1)
                    elif kind == "E":
                        exponentials(part, *args)
                    elif kind == "O":
                        act.wait_ge(o_full, part.g * NT + args[0] + 1)
                        nc.scalar.copy(oT[0][:], psO).then_inc(o_hi, 1)
                    elif kind in ("center_y", "norm_y", "center_x1", "norm_x1"):
                        norms(kind, *args)

            def silu_gate(n, slot):
                act.wait_ge(gu_full, n + 1)
                nc.scalar.activation(g_sb[:, slot, :], psS[:, slot, 0:CW], ACT.Silu).then_inc(g_done, 1)

            def hi_of_hidden(n, slot):
                act.wait_ge(ht_full, n + 1)
                nc.scalar.copy(hT[0][:, slot, :], psS[:, slot, BANK:BANK + CW]).then_inc(ht_hi, 1)

            attention(prologue())
            with act.Fori(0, G - 1) as g:
                attention(group(g))
            attention(last_group())
            for n in range(NT + 1):
                if n >= 1:
                    silu_gate(n - 1, (n - 1) % 2)
                for i in ((0, 1) if n == 0 else (n + 1,)):
                    if i < NT:
                        hi_of_turn(tile_of(xn1T[0], ORDER[i]), psT[:, i % 2, :], T_ATT + i + 1)
                if n < 2:
                    norms("center_y", NT - 2 + n)
                    norms("norm_y", NT - 2 + n)
                if n < 3:
                    norms("center_x1", NT - 3 + n)
                    norms("norm_x1", NT - 3 + n)
                if n >= 2:
                    hi_of_hidden(n - 2, n % 2)
            with act.Fori(0, (C - 1) // 2) as r:
                for m in range(2 * NT):
                    n = (2 * NT) * r + NT + m
                    silu_gate(n, m % 2)
                    hi_of_hidden(n - 1, (m - 1) % 2)
            hi_of_hidden(C * NT - 1, (C * NT - 1) % 2)

        @block.vector
        def _(dve):
            own = [0]

            def link(instruction):
                own[0] += 1
                instruction.then_inc(own_step, 1)
                dve.wait_ge(own_step, own[0])

            def lo_part(dst, psum, hi):
                return nc.vector.tensor_tensor(dst, psum, hi.bitcast(F32), ALU.subtract)

            def lo_of_turn(parts, bank, count):
                dve.wait_ge(t_hi, count)
                src = bank[:, 0:free_size(parts[1])]
                if len(parts[1].shape) == 3:
                    src = src.rearrange("p (a b) -> p a b", b=P)
                lo_part(parts[1], src, parts[0]).then_inc(t_done, 1)

            def masked_max(part, s, h):
                dve.wait_ge(s_full, softmax_count(part, s, h))
                dve.sem_inc(dve_passed, 1)
                cols, at = (ORDER[s] + 1) * P, score_offset(ORDER[s])
                nc.vector.tensor_tensor_reduce(out=probs[:, h, 0:cols], in0=psS[:, h % 2, at:at + cols],
                                               in1=mask[:, S - cols:S], scale=-SCALE, scalar=-NEG,
                                               op0=ALU.add, op1=ALU.min,
                                               accum_out=negmax[:, h:h + 1]).then_inc(s_done, 1)

            def add_projection(part, s):
                dve.wait_ge(y_full, part.g * NT + s + 1)
                tile = y[:, ORDER[s], :]
                nc.vector.tensor_tensor(tile, psY, tile, ALU.add).then_inc(y_done, 1)

            def attention(part):
                for item in part.items:
                    kind, *args = item
                    if kind == "X":
                        i = args[0]
                        if i < TPB - 1:
                            normalise_x(i + 1)
                        if i < TPB - 2:
                            x_statistics(i + 2)
                    if kind == "VT":
                        dve.wait_ge(t_full, part.use(item) + 1)
                        nc.vector.tensor_copy(vt[:], part.place(item)).then_inc(t_done, 1)
                    elif item in part.copy:
                        lo_of_turn(turned(item), part.place(item), part.hi(item))
                        if item == ("X", TPB - 1):
                            dve.wait_ge(w0_hi, KT)
                            lo_part(w[1][:, KT - 1, :], raw_w[:, KT - 1, :], w[0][:, KT - 1, :]).then_inc(w_ready, 1)
                            for k in range(TPB, NT):
                                x_statistics(k)
                                if k > TPB:
                                    normalise_x(k - 1)
                            normalise_x(NT - 1)
                    elif kind == "S":
                        masked_max(part, *args)
                    elif kind == "E":
                        dve.wait_ge(e_done, softmax_count(part, *args))
                        h = args[1]
                        nc.vector.reciprocal(rsum[:, h:h + 1], lsum[:, h:h + 1]).then_inc(r_done, 1)
                    elif kind == "A":
                        add_projection(part, *args)
                    elif kind == "O":
                        dve.wait_ge(o_hi, part.g * NT + args[0] + 1)
                        lo_part(oT[1][:], psO, oT[0][:]).then_inc(o_done, 1)
                    elif kind == "stat_y":
                        output_statistics(*args)
                    elif kind == "residual":
                        residual(*args)
                    elif kind == "stat_x1":
                        residual_statistics(*args)
                    elif kind == "scales":
                        tile_scales(*args)

            def statistics(src, s, means, done, negmean=None):
                link(nc.vector.bn_stats(st[:, s % 2, :], src))
                link(nc.vector.bn_aggr(means[:, s, :], st[:, s % 2, :]))
                if negmean is not None:
                    nc.vector.tensor_scalar(negmean[:, s:s + 1], means[:, s, 0:1], -1.0, None, ALU.mult)
                nc.vector.tensor_scalar(means[:, s, 1:2], means[:, s, 1:2], EPS, None, ALU.add).then_inc(done, 1)

            def normalise(dst, src, means, rs, s):
                return nc.vector.tensor_scalar(dst, src, means[:, s, 0:1], rs[:, s:s + 1], ALU.subtract, ALU.mult)

            def x_statistics(i):
                dve.wait_ge(x_in[i], 16)
                statistics(xt[:, i, :], i, mv, stat_x)

            def normalise_x(i):
                dve.wait_ge(rstd_x, i + 1)
                normalise(xt[:, i, :], xt[:, i, :], mv, rstd, i).then_inc(xn_ready, 1)

            def output_statistics(s):
                dve.wait_ge(y_done, (G - 1) * NT + s + 2)
                statistics(y[:, ORDER[s], :], s, mv, stat_y, nmean)

            def residual(s):
                i = ORDER[s]
                dve.wait_ge(x_in[i], 32)
                dve.wait_ge(yn_ready, s + 1)
                link(nc.vector.tensor_tensor(x1[:, i, :], x1[:, i, :], y[:, i, :], ALU.add))

            def residual_statistics(s):
                i = ORDER[s]
                statistics(x1[:, i, :], s, mv1, stat_x1, nmean1)

            def tile_scales(s):
                slot = s % 2
                dve.wait_ge(x1n_ready, s + 1)
                if s >= 2:
                    dve.wait_ge(xn1_ready, s - 1)
                link(block_max(y[:, ORDER[s], :], amax[:, slot, :]))
                link(block_scale(qs[:, slot, :], amax[:, slot, :]))
                nc.vector.reciprocal(qr[:, slot, :], qs[:, slot, :]).then_inc(scaled, 1)

            def block_max(src, mx):
                return nc.vector.tensor_reduce(mx, src.rearrange("p (n c) -> p n c", c=P), AXX, ALU.max,
                                               apply_absolute_value=True)

            def block_scale(scale, mx):
                return nc.vector.tensor_scalar(scale, mx, 1.0 / FP8_MAX, SCALE_FLOOR, ALU.mult, ALU.add)

            def make_hidden(n, slot):
                dve.wait_ge(g_done, n + 1)
                nc.vector.tensor_tensor(h_sb[:, slot, :], psS[:, slot, CW:2 * CW], g_sb[:, slot, :],
                                        ALU.mult).then_inc(h_made, 1)
                dve.wait_ge(h_made, n + 1)
                block_max(h_sb[:, slot, :], hmax[:, slot, :]).then_inc(h_step, 1)
                dve.wait_ge(h_step, 2 * n + 1)
                block_scale(hs[:, slot, :], hmax[:, slot, :]).then_inc(h_step, 1)
                dve.wait_ge(h_step, 2 * n + 2)
                nc.vector.reciprocal(hr[:, slot, :], hs[:, slot, :]).then_inc(h_scaled, 1)

            def lo_of_hidden(n, slot):
                dve.wait_ge(ht_hi, n + 1)
                lo_part(hT[1][:, slot, :], psS[:, slot, BANK:BANK + CW], hT[0][:, slot, :]).then_inc(ht_done, 1)

            def add_down(n, s, first):
                dve.wait_ge(d_full, n + 1)
                tile, bank = y[:, ORDER[s], :], psOY[:, s % 2, :]
                if first:
                    nc.vector.tensor_copy(tile, bank).then_inc(d_done, 1)
                else:
                    nc.vector.tensor_tensor(tile, bank, tile, ALU.add).then_inc(d_done, 1)

            dve.sem_inc(s_done, 2)
            dve.sem_inc(o_done, 1)
            dve.sem_inc(y_done, 1)
            x_statistics(0)
            x_statistics(1)
            normalise_x(0)
            dve.wait_ge(const_ready, 5)
            attention(prologue())
            dve.wait_ge(const_ready, 6)
            with dve.Fori(0, G - 1) as g:
                attention(group(g))
            attention(last_group())
            for n in range(NT + 1):
                if n >= 1:
                    make_hidden(n - 1, (n - 1) % 2)
                for i in ((0, 1) if n == 0 else (n + 1,)):
                    if i < NT:
                        lo_of_turn([tile_of(t, ORDER[i]) for t in xn1T], psT[:, i % 2, :], H_ATT + i + 1)
                    if NT - 2 <= i < NT:
                        link(nc.vector.memset(y[:, ORDER[i], :], 0.0))
                if n == 0:
                    add_projection(last_group(), NT - 1)
                    output_statistics(NT - 1)
                if n >= 2:
                    lo_of_hidden(n - 2, n % 2)
                if n < 4:
                    tile_scales(NT - 4 + n)
                if n < 2:
                    residual(NT - 2 + n)
                    residual_statistics(NT - 2 + n)
                if n >= 3:
                    add_down(n - 3, n - 3, True)

            def feed_forward_step(n, m):
                make_hidden(n, m % 2)
                lo_of_hidden(n - 1, (m - 1) % 2)
                add_down(n - 2, (m - 2) % NT, False)

            def finish(s):
                if s < NT:
                    dve.wait_ge(d_done, (C - 1) * NT + s + 1)
                    statistics(y[:, ORDER[s], :], s, mv, stat_fin)
                if s >= 1:
                    tile = y[:, ORDER[s - 1], :]
                    dve.wait_ge(rstd_fin, s)
                    normalise(tile, tile, mv, rstd, s - 1).then_inc(z_ready, 1)
                if s == NT:
                    dve.wait_ge(z_ready, NT)
                    nc.vector.tensor_tensor(x1[:, ORDER[s - 1], :], x1[:, ORDER[s - 1], :], tile,
                                            ALU.add).then_inc(last_ready, 1)

            with dve.Fori(0, (C - 3) // 2) as r:
                for m in range(2 * NT):
                    feed_forward_step((2 * NT) * r + NT + m, m)
            for m in range(2 * NT):
                feed_forward_step((C - 2) * NT + m, m)
                if m == 2 * NT - 1:
                    lo_of_hidden(C * NT - 1, 1)
                if m - 2 >= NT:
                    finish(m - 2 - NT)
            for s in (NT - 2, NT - 1):
                add_down((C - 1) * NT + s, s, False)
                finish(s)
            finish(NT)

        @block.tensor
        def _(pe):
            def product(dst, pieces, **flags):
                terms = [t for lhs, rhs in pieces for t in split_passes(lhs, rhs)]
                for k, (a, b) in enumerate(terms):
                    last = nc.tensor.matmul(dst, a, b, start=(k == 0), stop=(k == len(terms) - 1))
                return last

            def turn_bank(part, item):
                if not part.first:
                    pe.wait_ge(t_done, part.use(item) - 1)
                elif part.before(item):
                    pe.wait_ge(t_done, part.before(item))
                return part.place(item)

            def project(part, item, col, half, first=False):
                bank = turn_bank(part, item)
                for m in range(KT):
                    if first and (m == 0 or not part.first):
                        pe.wait_ge(w_ready, KT if part.first else (part.g + 1) * KT + m + 1)
                    terms = split_passes([t[:, m, col:col + P] for t in w],
                                         [t[:, m, half * BANK:(half + 1) * BANK] for t in xnT])
                    for k, (a, b) in enumerate(terms):
                        last = nc.tensor.matmul(bank, a, b, start=(m == 0 and k == 0), stop=(m == KT - 1 and k == 2))
                last.then_inc(t_full, 1)

            def turn_tile(bank, src, ready, count):
                pe.wait_ge(ready, count)
                for m in range(KT):
                    last = nc.tensor.transpose(bank[:, m * P:(m + 1) * P], src[:, m * P:(m + 1) * P], ident[:])
                last.then_inc(t_full, 1)

            def turn_values(part, item):
                bank = turn_bank(part, item)
                pe.wait_ge(t_done, part.use(("VT", item[1])) + 1)
                for m in range(TPB):
                    last = nc.tensor.transpose(bank[:, m * P:(m + 1) * P], vt[:, m * P:(m + 1) * P], ident[:])
                last.then_inc(t_full, 1)

            def scores(part, s, h):
                i = ORDER[s]
                if s == 0 and h == 0:
                    pe.wait_ge(t_done, part.use(("Q", 0, HG - 1)) + 1)
                if s == 1:
                    pe.wait_ge(t_done, part.uses - behind(("Q", 1, h)))
                pe.wait_ge(s_done, softmax_count(part, s, h))
                at, key = score_offset(i), 0
                while key < (i + 1) * P:
                    cols = max(2 * P, min(BANK - (at + key) % BANK, (i + 1) * P - key))
                    last = product(psS[:, h % 2, at + key:at + key + cols],
                                   [([t[:, h, i * P:(i + 1) * P] for t in qT], [t[:, key:key + cols] for t in kT])])
                    key += cols
                last.then_inc(s_full, 1)

            def turn_probs(part, item):
                _, s, b, h = item
                bank = turn_bank(part, item)
                if b == 0:
                    pe.wait_ge(p_ready, part.g * (NT * HG) + s * HG + h + 1)
                for j in range(b * TPB, min((b + 1) * TPB, ORDER[s] + 1)):
                    last = nc.tensor.transpose(bank[:, (j % TPB) * P:(j % TPB + 1) * P],
                                               probs[:, h, j * P:(j + 1) * P], ident[:])
                last.then_inc(t_full, 1)

            def weighted_values(part, s, j):
                if j == 0:
                    pe.wait_ge(o_done, part.g * NT + s + 1)
                if j % TPB == 0:
                    pe.wait_ge(t_done, part.use(("P", s, j // TPB, HG - 1)) + 1)
                for k, (a, b) in enumerate(split_passes([t[:, j, :] for t in v], [t[:, j, :] for t in pT])):
                    last = nc.tensor.matmul(psO, a, b, start=(j == 0 and k == 0), stop=(j == ORDER[s] and k == 2))
                if j == ORDER[s]:
                    last.then_inc(o_full, 1)

            def output_share(part, s, h):
                g = part.g
                if h == 0:
                    pe.wait_ge(o_done, g * NT + s + 2)
                    pe.wait_ge(y_done, g * NT + s + 1)
                    if s == 0:
                        pe.wait_ge(wd_ready, g * HG + HG)
                terms = split_passes([t[:, h * P:(h + 1) * P] for t in oT], [t[:, h, :] for t in wd])
                for k, (a, b) in enumerate(terms):
                    last = nc.tensor.matmul(psY, a, b, start=(h == 0 and k == 0), stop=(h == HG - 1 and k == 2))
                if h == HG - 1:
                    last.then_inc(y_full, 1)

            def attention(part):
                for item in part.items:
                    kind, *args = item
                    if kind == "X":
                        turn_tile(turn_bank(part, item), xt[:, args[0], :], xn_ready, args[0] + 1)
                    elif kind == "K":
                        if part.first:
                            pe.wait_ge(t_done, part.use(("X", (args[0] + 1) * TPB - 1)) + 1)
                        project(part, item, K_COL, args[0], first=(args[0] == 0))
                    elif kind == "VT":
                        project(part, item, V_COL, args[0])
                    elif kind == "Q":
                        project(part, item, args[1] * P, args[0])
                    elif kind == "V":
                        turn_values(part, item)
                    elif kind == "S":
                        scores(part, *args)
                    elif kind == "P":
                        turn_probs(part, item)
                    elif kind == "PV":
                        weighted_values(part, *args)
                    elif kind == "Y":
                        output_share(part, *args)

            def gate_up(n, slot, i, up):
                if not isinstance(n, int) or n >= 2:
                    pe.wait_ge(h_made, n - 1)
                product(psS[:, slot, 0:BANK], [([t[:, m, i * P:(i + 1) * P] for t in xn1T], [t[:, m, :] for t in up])
                                               for m in range(KT)]).then_inc(gu_full, 1)

            def turn_hidden(n, slot):
                pe.wait_ge(h_ready, n + 1)
                if not isinstance(n, int) or n >= 2:
                    pe.wait_ge(ht_done, n - 1)
                for m in range(CB):
                    last = nc.tensor.transpose(psS[:, slot, BANK + m * P:BANK + (m + 1) * P],
                                               h_sb[:, slot, m * P:(m + 1) * P], ident[:])
                last.then_inc(ht_full, 1)

            def down(n, slot, weights):
                pe.wait_ge(ht_done, n + 1)
                if not isinstance(n, int) or n >= 2:
                    pe.wait_ge(d_done, n - 1)
                product(psOY[:, slot, :], [([t[:, slot, m * P:(m + 1) * P] for t in hT],
                                            [t[:, weights * CB + m, :] for t in down_w])
                                           for m in range(CB)]).then_inc(d_full, 1)

            up_place = [[t[:, :, 0:2 * CW] for t in w], [t[:, :, 0:2 * CW] for t in qT]]

            pe.wait_ge(const_ready, 4)
            attention(prologue())
            with pe.Fori(0, G - 1) as g:
                attention(group(g))
            attention(last_group())
            for n in range(NT + 1):
                if n >= 1:
                    if n == 1:
                        pe.wait_ge(up_ready, KT)
                        pe.wait_ge(s_done, G * NT * HG + 2)
                    pe.wait_ge(t_done, T_ATT + n)
                    gate_up(n - 1, (n - 1) % 2, ORDER[n - 1], up_place[0])
                for i in ((0, 1) if n == 0 else (n + 1,)):
                    if i < NT:
                        pe.wait_ge(t_done, T_ATT + i - 1)
                        turn_tile(psT[:, i % 2, :], y[:, ORDER[i], :], xn1_ready, i + 1)
                if n == 0:
                    for h in range(HG):
                        output_share(last_group(), NT - 1, h)
                if n >= 3:
                    if n == 3:
                        pe.wait_ge(down_ready, CB)
                        pe.wait_ge(y_done, G * NT + 1)
                    down(n - 3, (n - 3) % 2, 0)
                if n >= 2:
                    turn_hidden(n - 2, n % 2)
            with pe.Fori(0, (C - 1) // 2) as r:
                for m in range(2 * NT):
                    n = (2 * NT) * r + NT + m
                    parity = (m // NT + 1) % 2
                    if m % NT == 0:
                        pe.wait_ge(up_ready, (2 * KT) * r + (2 + m // NT) * KT)
                    gate_up(n, m % 2, ORDER[m % NT], up_place[parity])
                    if m % NT == 2:
                        pe.wait_ge(down_ready, (2 * CB) * r + (2 + m // NT) * CB)
                    down(n - 2, m % 2, parity if m % NT >= 2 else 1 - parity)
                    turn_hidden(n - 1, (m - 1) % 2)
            turn_hidden(C * NT - 1, 1)
            down(C * NT - 2, 0, (C - 1) % 2)
            down(C * NT - 1, 1, (C - 1) % 2)


def kernel(L0_attn_q, L0_attn_w_qkv, L0_attn_w_dense, L0_ffn_w1, L0_ffn_w1_scale, L0_ffn_w3, L0_ffn_w3_scale,
           L0_ffn_w2, L0_ffn_w2_scale):
    import concourse.bacc as bacc
    import numpy as np
    from concourse.bass_utils import run_bass_kernel_spmd

    x = np.ascontiguousarray(L0_attn_q)[0]
    S, D = x.shape
    KT, G, HG, C = D // P, 8, 4, 7
    qkv, wd = np.ascontiguousarray(L0_attn_w_qkv), np.ascontiguousarray(L0_attn_w_dense)
    nq, nkv = G * HG * P, G * P
    rows = np.concatenate([qkv[:nq].reshape(G, HG * P, D), qkv[nq:nq + nkv].reshape(G, P, D),
                           qkv[nq + nkv:].reshape(G, P, D)], axis=1)
    w_attn = rows.reshape(G, (HG + 2) * P, KT, P).transpose(0, 3, 2, 1)
    w_dense = wd.reshape(D, G, HG, P).transpose(1, 3, 2, 0)
    w1, w3, w2 = (np.ascontiguousarray(a) for a in (L0_ffn_w1, L0_ffn_w3, L0_ffn_w2))
    F = w1.shape[0]
    CW = F // C
    CB = CW // P
    w_up = np.concatenate([a.reshape(C, CW, KT, P).transpose(0, 3, 2, 1) for a in (w1, w3)], axis=3)
    w_down = w2.reshape(D, C, CB, P).transpose(1, 3, 2, 0)
    s1, s3, s2 = (np.ascontiguousarray(a) for a in (L0_ffn_w1_scale, L0_ffn_w3_scale, L0_ffn_w2_scale))
    s_up = np.concatenate([a.reshape(C, CB, KT).transpose(0, 2, 1) for a in (s1, s3)], axis=2).reshape(1, -1)
    s_down = s2.reshape(D // P, C, CB).transpose(1, 2, 0).reshape(1, -1)

    nc = bacc.Bacc("TRN2", target_bir_lowering=False, num_devices=1)
    arrays, args = {}, []
    for name, a in (("x", x), ("w_attn", w_attn), ("w_dense", w_dense), ("w_up", w_up), ("w_down", w_down),
                    ("s_up", s_up), ("s_down", s_down)):
        arrays[f"in_{name}"] = np.ascontiguousarray(a)
        args.append(nc.dram_tensor(f"in_{name}", a.shape, F32, kind="ExternalInput").ap())
    args.append(nc.dram_tensor("result", (S, D), F32, kind="ExternalOutput").ap())
    sandwich_kernel(nc, *args)
    r = run_bass_kernel_spmd(nc, [arrays], core_ids=[0])
    return r.results[0]["result"].reshape(1, S, D)
```
